# Optimizing a Trainium2 kernel written in Bass

```python
import numpy as np
import jax
import jax.numpy as jnp

def _softmax(x, axis=-1):
    return jax.nn.softmax(x, axis=axis)

def _gelu(x):
    return jax.nn.gelu(x, approximate=True)

def _silu(x):
    return jax.nn.silu(x)

def _sigmoid(x):
    return jax.nn.sigmoid(x)

def _layernorm(x, axis=-1, eps=1e-05):
    m = jnp.mean(x, axis=axis, keepdims=True)
    v = jnp.var(x, axis=axis, keepdims=True)
    return (x - m) / jnp.sqrt(v + eps)

def _scatter_add(tgt, idx, src, axis=0):
    return tgt.at[idx].add(src)

def _segment_sum(src, seg, n):
    return jax.ops.segment_sum(src, seg, n)
kernel_name = 'mk_vit_tower_postln_d4_tok_img256_r4_822c09'

def setup_inputs(seed: int=0):
    np.random.seed(seed)
    _w = jnp.asarray

    def _rec_inputs():
        import jax
        import jax.numpy as jnp
        _rk = jax.random.key(seed)
        x = -0.000222058 + 0.999998 * jax.random.normal(jax.random.fold_in(_rk, 1), (16, 3, 96, 96), jnp.float32)
        return x
    x = _rec_inputs()

    def _L0_tok_setup():
        import jax, jax.numpy as jnp
        import numpy as np
        IMAGE_SIZE = 64
        PATCH = 16
        EMBED_DIM = 64
        IN_CH = 3
        BATCH = 128
        IN_DIM = IN_CH * PATCH * PATCH

        def _patchify(x, p):
            B, C, H, Wd = x.shape
            x = x.reshape(B, C, H // p, p, Wd // p, p)
            x = x.transpose(0, 2, 4, 1, 3, 5)
            return x.reshape(B, H // p * (Wd // p), C * p * p)
        key = jax.random.key(seed)
        kx, kw, kb = jax.random.split(key, 3)
        x = jax.random.normal(kx, (BATCH, IN_CH, IMAGE_SIZE, IMAGE_SIZE), dtype=jnp.float32)
        W = jax.random.normal(kw, (EMBED_DIM, IN_DIM), dtype=jnp.float32) * (1.0 / np.sqrt(IN_DIM))
        b = jax.random.normal(kb, (EMBED_DIM,), dtype=jnp.float32) * 0.01
        return {'x': x, 'W': W, 'b': b}
    _L0_tok_all = _L0_tok_setup()
    _L0_tok_in = {k: v for k, v in _L0_tok_all.items() if k in ('W', 'b')}
    del _L0_tok_all

    def _L0_attn_setup():
        import jax, jax.numpy as jnp
        import numpy as np
        D, S, E, MPE = (64, 128, 128, 1024)
        B, N = (2, 1024)

        def _rope(x):
            n, d = (x.shape[-2], x.shape[-1])
            half = d // 2
            pos = jnp.arange(n, dtype=x.dtype)
            inv_freq = 10000.0 ** (-jnp.arange(half, dtype=x.dtype) / half)
            sinusoid = pos[:, None] * inv_freq
            sin, cos = (jnp.sin(sinusoid), jnp.cos(sinusoid))
            x1, x2 = jnp.split(x, 2, axis=-1)
            return jnp.concatenate([x1 * cos - x2 * sin, x2 * cos + x1 * sin], axis=-1)
        key = jax.random.key(seed)
        ks = jax.random.split(key, 12)
        std = 0.02
        return {'query': jax.random.normal(ks[0], (B, N, D), jnp.float32), 'ln_w': jnp.ones((D,), jnp.float32), 'ln_b': jnp.zeros((D,), jnp.float32), 'Wu': jax.random.normal(ks[1], (D, E), jnp.float32) / np.float32(np.sqrt(D)), 'bu': jnp.zeros((E,), jnp.float32), 'Wv': jax.random.normal(ks[2], (D, E), jnp.float32) / np.float32(np.sqrt(D)), 'bv': jnp.zeros((E,), jnp.float32), 'Wbase': jax.random.normal(ks[3], (D, S), jnp.float32) / np.float32(np.sqrt(D)), 'bbase': jnp.zeros((S,), jnp.float32), 'q_w': jax.random.normal(ks[4], (1, S), jnp.float32) * std, 'q_b': jnp.zeros((1, S), jnp.float32), 'k_w': jax.random.normal(ks[5], (1, S), jnp.float32) * std, 'k_b': jnp.zeros((1, S), jnp.float32), 'w_rel': jax.random.normal(ks[6], (2 * MPE - 1,), jnp.float32) * std, 'Wo': jax.random.normal(ks[7], (E, D), jnp.float32) / np.float32(np.sqrt(E)), 'bo': jnp.zeros((D,), jnp.float32)}
    _L0_attn_all = _L0_attn_setup()
    _L0_attn_in = {k: v for k, v in _L0_attn_all.items() if k in ('ln_w', 'ln_b', 'Wu', 'bu', 'Wv', 'bv', 'Wbase', 'bbase', 'q_w', 'q_b', 'k_w', 'k_b', 'w_rel', 'Wo', 'bo')}
    del _L0_attn_all

    def _L0_ffn_setup():
        import math
        import jax, jax.numpy as jnp
        import numpy as np
        CAPACITY_FACTOR = 1.25
        key = jax.random.key(seed)
        ks = jax.random.split(key, 5)
        B, L, D, F, E = (8, 2048, 64, 256, 8)
        h = jax.random.normal(ks[0], (B, L, D), dtype=jnp.float32)
        gate_w = jax.random.normal(ks[1], (D, E), dtype=jnp.float32) * 0.02
        gate_b = jnp.zeros((E,), dtype=jnp.float32)
        w1 = jax.random.normal(ks[2], (E, D, F), dtype=jnp.float32) * (1.0 / math.sqrt(D))
        b1 = jnp.zeros((E, F), dtype=jnp.float32)
        w2 = jax.random.normal(ks[3], (E, F, D), dtype=jnp.float32) * (1.0 / math.sqrt(F))
        b2 = jnp.zeros((E, D), dtype=jnp.float32)
        return {'h': h, 'gate_w': gate_w, 'gate_b': gate_b, 'w1': w1, 'b1': b1, 'w2': w2, 'b2': b2}
    _L0_ffn_all = _L0_ffn_setup()
    _L0_ffn_in = {k: v for k, v in _L0_ffn_all.items() if k in ('gate_w', 'gate_b', 'w1', 'b1', 'w2', 'b2')}
    del _L0_ffn_all

    def _L1_attn_setup():
        import jax, jax.numpy as jnp
        import numpy as np
        import math
        STATE_DIM = 64
        R_MIN, R_MAX = (0.4, 0.9)
        PHASE_MAX = 2.0 * math.pi
        BATCH, SEQ = (8, 1024)

        def _binop(e_i, e_j):
            a_i, b_i = e_i
            a_j, b_j = e_j
            return (a_j * a_i, a_j * b_i + b_j)
        key = jax.random.key(seed)
        k_x, k_u1, k_u2, k_br, k_bi, k_cr, k_ci = jax.random.split(key, 7)
        D = STATE_DIM
        x = jax.random.normal(k_x, (BATCH, SEQ, D), dtype=jnp.float32)
        u1 = jax.random.uniform(k_u1, (D,), dtype=jnp.float32)
        nu_log = jnp.log(-0.5 * jnp.log(u1 * (R_MAX + R_MIN) * (R_MAX - R_MIN) + R_MIN ** 2))
        u2 = jax.random.uniform(k_u2, (D,), dtype=jnp.float32)
        theta_log = jnp.log(PHASE_MAX * u2)
        lam_mod = jnp.exp(-jnp.exp(nu_log))
        gamma_log = jnp.log(jnp.sqrt(1.0 - jnp.square(lam_mod)))
        s_b = 1.0 / math.sqrt(2 * D)
        s_c = 1.0 / math.sqrt(D)
        B_re = jax.random.normal(k_br, (D, D), dtype=jnp.float32) * s_b
        B_im = jax.random.normal(k_bi, (D, D), dtype=jnp.float32) * s_b
        C_re = jax.random.normal(k_cr, (D, D), dtype=jnp.float32) * s_c
        C_im = jax.random.normal(k_ci, (D, D), dtype=jnp.float32) * s_c
        return {'x': x, 'nu_log': nu_log, 'theta_log': theta_log, 'gamma_log': gamma_log, 'B_re': B_re, 'B_im': B_im, 'C_re': C_re, 'C_im': C_im}
    _L1_attn_all = _L1_attn_setup()
    _L1_attn_in = {k: v for k, v in _L1_attn_all.items() if k in ('nu_log', 'theta_log', 'gamma_log', 'B_re', 'B_im', 'C_re', 'C_im')}
    del _L1_attn_all

    def _L1_ffn_setup():
        import jax, jax.numpy as jnp
        import numpy as np
        NUM_EXPERTS = 8
        TOP_K = 2
        B, S, D = (8, 2048, 64)

        def _moe(tokens, router_w, w1, b1, w2, b2):
            N = tokens.shape[0]
            E = router_w.shape[0]
            logits = tokens.astype(jnp.float32) @ router_w.astype(jnp.float32).T
            probs = jax.nn.softmax(logits, axis=-1)
            rw, re = jax.lax.top_k(probs, TOP_K)
            if TOP_K > 1:
                rw = rw / jnp.maximum(rw.sum(-1, keepdims=True), 1e-12)
            rw = rw.astype(tokens.dtype)
            combine = jnp.zeros((N, E), tokens.dtype).at[jnp.arange(N)[:, None], re].set(rw)
            out = tokens
            for e in range(E):
                h = jax.nn.gelu(tokens @ w1[e] + b1[e], approximate=False)
                y = h @ w2[e] + b2[e]
                out = out + combine[:, e:e + 1] * y
            return out
        key = jax.random.key(seed)
        ks = jax.random.split(key, 4)
        scale = 1.0 / np.sqrt(D).astype(np.float32)
        return {'input_embeddings': jax.random.normal(ks[0], (B, S, D), jnp.float32), 'router_w': jax.random.normal(ks[1], (NUM_EXPERTS, D), jnp.float32) * scale, 'w1': jax.random.normal(ks[2], (NUM_EXPERTS, D, D), jnp.float32) * scale, 'b1': jnp.zeros((NUM_EXPERTS, D), jnp.float32), 'w2': jax.random.normal(ks[3], (NUM_EXPERTS, D, D), jnp.float32) * scale, 'b2': jnp.zeros((NUM_EXPERTS, D), jnp.float32)}
    _L1_ffn_all = _L1_ffn_setup()
    _L1_ffn_in = {k: v for k, v in _L1_ffn_all.items() if k in ('router_w', 'w1', 'b1', 'w2', 'b2')}
    del _L1_ffn_all

    def _L2_attn_setup():
        import jax, jax.numpy as jnp
        import numpy as np
        H = 4
        TOP_K = 8
        CAUSAL = True
        W_STD = 0.04
        key = jax.random.key(seed)
        kx, kq, kk, kv, ko = jax.random.split(key, 5)
        B, T, d = (2, 128, 64)
        x = jax.random.normal(kx, (B, T, d), dtype=jnp.float32)
        Wq = jax.random.normal(kq, (d, d), dtype=jnp.float32) * W_STD
        Wk = jax.random.normal(kk, (d, d), dtype=jnp.float32) * W_STD
        Wv = jax.random.normal(kv, (d, d), dtype=jnp.float32) * W_STD
        Wo = jax.random.normal(ko, (d, d), dtype=jnp.float32) * W_STD
        return {'x': x, 'Wq': Wq, 'Wk': Wk, 'Wv': Wv, 'Wo': Wo}
    _L2_attn_all = _L2_attn_setup()
    _L2_attn_in = {k: v for k, v in _L2_attn_all.items() if k in ('Wq', 'Wk', 'Wv', 'Wo')}
    del _L2_attn_all

    def _L2_ffn_setup():
        import jax, jax.numpy as jnp
        import numpy as np
        E = 8
        K = 2
        D = 64
        H = 128
        DOUT = 64
        EPS = 1e-05
        key = jax.random.key(seed)
        ks = jax.random.split(key, 9)
        s = 0.02
        return {'x': jax.random.normal(ks[0], (4, 2048, D), jnp.float32), 'gamma': 1.0 + 0.05 * jax.random.normal(ks[1], (D,), jnp.float32), 'beta': 0.05 * jax.random.normal(ks[2], (D,), jnp.float32), 'Wr': 0.01 * jax.random.normal(ks[3], (D, E), jnp.float32), 'br': jnp.zeros((E,), jnp.float32), 'W1': s * jax.random.normal(ks[4], (E, D, H), jnp.float32), 'b1': s * jax.random.normal(ks[5], (E, H), jnp.float32), 'W2': s * jax.random.normal(ks[6], (E, H, DOUT), jnp.float32), 'b2': s * jax.random.normal(ks[7], (E, DOUT), jnp.float32)}
    _L2_ffn_all = _L2_ffn_setup()
    _L2_ffn_in = {k: v for k, v in _L2_ffn_all.items() if k in ('gamma', 'beta', 'Wr', 'br', 'W1', 'b1', 'W2', 'b2')}
    del _L2_ffn_all

    def _L3_attn_setup():
        import jax, jax.numpy as jnp
        import numpy as np
        key = jax.random.key(seed)
        k1, k2 = jax.random.split(key)
        B, N, F = (4, 1024, 64)
        nodes = jax.random.normal(k1, (B, N, F), dtype=jnp.float32)
        limit = np.sqrt(6.0 / (F + F)).astype(np.float32)
        W = jax.random.uniform(k2, (F, F), dtype=jnp.float32, minval=-limit, maxval=limit)
        return {'nodes': nodes, 'W': W}
    _L3_attn_all = _L3_attn_setup()
    _L3_attn_in = {k: v for k, v in _L3_attn_all.items() if k in ('W',)}
    del _L3_attn_all

    def _L3_ffn_setup():
        import jax, jax.numpy as jnp
        import numpy as np
        C = 64
        HID = 256
        E = 8
        TEMP = 1.0
        key = jax.random.key(seed)
        ks = jax.random.split(key, 7)
        x = jax.random.normal(ks[0], (8, 4096, C), dtype=jnp.float32)
        W1 = jax.random.normal(ks[1], (C, HID), dtype=jnp.float32) * 0.02
        b1 = jnp.zeros((HID,), dtype=jnp.float32)
        Wg = jax.random.normal(ks[2], (HID, E), dtype=jnp.float32) * 0.02
        bg = jnp.zeros((E,), dtype=jnp.float32)
        Wd = jax.random.normal(ks[3], (E, HID, C), dtype=jnp.float32) * 0.02
        bd = jnp.zeros((E, C), dtype=jnp.float32)
        return {'x': x, 'W1': W1, 'b1': b1, 'Wg': Wg, 'bg': bg, 'Wd': Wd, 'bd': bd}
    _L3_ffn_all = _L3_ffn_setup()
    _L3_ffn_in = {k: v for k, v in _L3_ffn_all.items() if k in ('W1', 'b1', 'Wg', 'bg', 'Wd', 'bd')}
    del _L3_ffn_all
    return {'x': x, 'L0_tok_W': _L0_tok_in['W'], 'L0_tok_b': _L0_tok_in['b'], 'L0_attn_ln_w': _L0_attn_in['ln_w'], 'L0_attn_ln_b': _L0_attn_in['ln_b'], 'L0_attn_Wu': _L0_attn_in['Wu'], 'L0_attn_bu': _L0_attn_in['bu'], 'L0_attn_Wv': _L0_attn_in['Wv'], 'L0_attn_bv': _L0_attn_in['bv'], 'L0_attn_Wbase': _L0_attn_in['Wbase'], 'L0_attn_bbase': _L0_attn_in['bbase'], 'L0_attn_q_w': _L0_attn_in['q_w'], 'L0_attn_q_b': _L0_attn_in['q_b'], 'L0_attn_k_w': _L0_attn_in['k_w'], 'L0_attn_k_b': _L0_attn_in['k_b'], 'L0_attn_w_rel': _L0_attn_in['w_rel'], 'L0_attn_Wo': _L0_attn_in['Wo'], 'L0_attn_bo': _L0_attn_in['bo'], 'L0_ffn_gate_w': _L0_ffn_in['gate_w'], 'L0_ffn_gate_b': _L0_ffn_in['gate_b'], 'L0_ffn_w1': _L0_ffn_in['w1'], 'L0_ffn_b1': _L0_ffn_in['b1'], 'L0_ffn_w2': _L0_ffn_in['w2'], 'L0_ffn_b2': _L0_ffn_in['b2'], 'L1_attn_nu_log': _L1_attn_in['nu_log'], 'L1_attn_theta_log': _L1_attn_in['theta_log'], 'L1_attn_gamma_log': _L1_attn_in['gamma_log'], 'L1_attn_B_re': _L1_attn_in['B_re'], 'L1_attn_B_im': _L1_attn_in['B_im'], 'L1_attn_C_re': _L1_attn_in['C_re'], 'L1_attn_C_im': _L1_attn_in['C_im'], 'L1_ffn_router_w': _L1_ffn_in['router_w'], 'L1_ffn_w1': _L1_ffn_in['w1'], 'L1_ffn_b1': _L1_ffn_in['b1'], 'L1_ffn_w2': _L1_ffn_in['w2'], 'L1_ffn_b2': _L1_ffn_in['b2'], 'L2_attn_Wq': _L2_attn_in['Wq'], 'L2_attn_Wk': _L2_attn_in['Wk'], 'L2_attn_Wv': _L2_attn_in['Wv'], 'L2_attn_Wo': _L2_attn_in['Wo'], 'L2_ffn_gamma': _L2_ffn_in['gamma'], 'L2_ffn_beta': _L2_ffn_in['beta'], 'L2_ffn_Wr': _L2_ffn_in['Wr'], 'L2_ffn_br': _L2_ffn_in['br'], 'L2_ffn_W1': _L2_ffn_in['W1'], 'L2_ffn_b1': _L2_ffn_in['b1'], 'L2_ffn_W2': _L2_ffn_in['W2'], 'L2_ffn_b2': _L2_ffn_in['b2'], 'L3_attn_W': _L3_attn_in['W'], 'L3_ffn_W1': _L3_ffn_in['W1'], 'L3_ffn_b1': _L3_ffn_in['b1'], 'L3_ffn_Wg': _L3_ffn_in['Wg'], 'L3_ffn_bg': _L3_ffn_in['bg'], 'L3_ffn_Wd': _L3_ffn_in['Wd'], 'L3_ffn_bd': _L3_ffn_in['bd']}

def reference(x, L0_tok_W, L0_tok_b, L0_attn_ln_w, L0_attn_ln_b, L0_attn_Wu, L0_attn_bu, L0_attn_Wv, L0_attn_bv, L0_attn_Wbase, L0_attn_bbase, L0_attn_q_w, L0_attn_q_b, L0_attn_k_w, L0_attn_k_b, L0_attn_w_rel, L0_attn_Wo, L0_attn_bo, L0_ffn_gate_w, L0_ffn_gate_b, L0_ffn_w1, L0_ffn_b1, L0_ffn_w2, L0_ffn_b2, L1_attn_nu_log, L1_attn_theta_log, L1_attn_gamma_log, L1_attn_B_re, L1_attn_B_im, L1_attn_C_re, L1_attn_C_im, L1_ffn_router_w, L1_ffn_w1, L1_ffn_b1, L1_ffn_w2, L1_ffn_b2, L2_attn_Wq, L2_attn_Wk, L2_attn_Wv, L2_attn_Wo, L2_ffn_gamma, L2_ffn_beta, L2_ffn_Wr, L2_ffn_br, L2_ffn_W1, L2_ffn_b1, L2_ffn_W2, L2_ffn_b2, L3_attn_W, L3_ffn_W1, L3_ffn_b1, L3_ffn_Wg, L3_ffn_bg, L3_ffn_Wd, L3_ffn_bd):
    import jax
    import jax.numpy as jnp

    def _L0_tok_ref(x, W, b):
        import jax, jax.numpy as jnp
        import numpy as np
        IMAGE_SIZE = 64
        PATCH = 16
        EMBED_DIM = 64
        IN_CH = 3
        BATCH = 128
        IN_DIM = IN_CH * PATCH * PATCH

        def _patchify(x, p):
            B, C, H, Wd = x.shape
            x = x.reshape(B, C, H // p, p, Wd // p, p)
            x = x.transpose(0, 2, 4, 1, 3, 5)
            return x.reshape(B, H // p * (Wd // p), C * p * p)
        patches = _patchify(x, PATCH)
        return jnp.einsum('bnk,ek->bne', patches, W) + b

    def _L0_attn_ref(query, ln_w, ln_b, Wu, bu, Wv, bv, Wbase, bbase, q_w, q_b, k_w, k_b, w_rel, Wo, bo):
        import jax, jax.numpy as jnp
        import numpy as np
        D, S, E, MPE = (64, 128, 128, 1024)
        B, N = (2, 1024)

        def _rope(x):
            n, d = (x.shape[-2], x.shape[-1])
            half = d // 2
            pos = jnp.arange(n, dtype=x.dtype)
            inv_freq = 10000.0 ** (-jnp.arange(half, dtype=x.dtype) / half)
            sinusoid = pos[:, None] * inv_freq
            sin, cos = (jnp.sin(sinusoid), jnp.cos(sinusoid))
            x1, x2 = jnp.split(x, 2, axis=-1)
            return jnp.concatenate([x1 * cos - x2 * sin, x2 * cos + x1 * sin], axis=-1)
        mpe = (w_rel.shape[0] + 1) // 2
        bsz, n, d = query.shape
        mu = query.mean(axis=-1, keepdims=True)
        var = ((query - mu) ** 2).mean(axis=-1, keepdims=True)
        x = (query - mu) * jax.lax.rsqrt(var + 1e-05) * ln_w + ln_b
        u = jax.nn.silu(x @ Wu + bu)
        v = jax.nn.silu(x @ Wv + bv)
        base = jax.nn.silu(x @ Wbase + bbase)
        q = _rope(base * q_w + q_b)
        k = _rope(base * k_w + k_b)
        qk = jnp.einsum('bms,bns->bmn', q, k)
        i = jnp.arange(n)
        bias = w_rel[mpe - 1 + i[None, :] - i[:, None]]
        kernel = jnp.square(jax.nn.relu(qk / mpe + bias))
        out = u * jnp.einsum('bmn,bne->bme', kernel, v) @ Wo + bo
        return out

    def _L0_ffn_ref(h, gate_w, gate_b, w1, b1, w2, b2):
        import math
        import jax, jax.numpy as jnp
        import numpy as np
        CAPACITY_FACTOR = 1.25
        B, L, D = h.shape
        E = gate_w.shape[1]
        T = B * L
        C = max(1, math.ceil(CAPACITY_FACTOR * T / E))
        x = h.reshape(T, D)
        logits = x @ gate_w + gate_b
        probs = jax.nn.softmax(logits, axis=-1)
        idx = jnp.argmax(probs, axis=-1)
        prb = jnp.take_along_axis(probs, idx[:, None], axis=1)[:, 0]
        one_hot = jax.nn.one_hot(idx, E, dtype=jnp.float32)
        pos = (jnp.cumsum(one_hot, axis=0) * one_hot).sum(-1).astype(jnp.int32) - 1
        kept = pos < C
        pos_safe = jnp.where(kept, pos, C)
        buf = jnp.zeros((E, C, D), dtype=h.dtype).at[idx, pos_safe].set(x, mode='drop')
        hmid = jax.nn.relu(jnp.einsum('ecd,edf->ecf', buf, w1) + b1[:, None, :])
        ybuf = jnp.einsum('ecf,efd->ecd', hmid, w2) + b2[:, None, :]
        pos_g = jnp.minimum(pos, C - 1)
        y_tok = ybuf[idx, pos_g] * (prb * kept)[:, None]
        y = y_tok.reshape(B, L, D)
        y = jnp.nan_to_num(y, nan=0.0, posinf=10000.0, neginf=-10000.0)
        return y

    def _L1_attn_ref(x, nu_log, theta_log, gamma_log, B_re, B_im, C_re, C_im):
        import jax, jax.numpy as jnp
        import numpy as np
        import math
        STATE_DIM = 64
        R_MIN, R_MAX = (0.4, 0.9)
        PHASE_MAX = 2.0 * math.pi
        BATCH, SEQ = (8, 1024)

        def _binop(e_i, e_j):
            a_i, b_i = e_i
            a_j, b_j = e_j
            return (a_j * a_i, a_j * b_i + b_j)
        L_mod = jnp.exp(-jnp.exp(nu_log))
        theta = jnp.exp(theta_log)
        L_diag = (L_mod * jnp.cos(theta) + 1j * L_mod * jnp.sin(theta)).astype(jnp.complex64)
        B = (B_re + 1j * B_im).astype(jnpp.complex64) if False else (B_re + 1j * B_im).astype(jnp.complex64)
        C = (C_re + 1j * C_im).astype(jnp.complex64)
        B_norm = B * jnp.exp(gamma_log)[:, None]
        B_elems = x.astype(jnp.complex64) @ B_norm.T
        L_elems = jnp.broadcast_to(L_diag, B_elems.shape)
        _, inner_states = jax.lax.associative_scan(_binop, (L_elems, B_elems), axis=1)
        return (inner_states @ C.T).real

    def _L1_ffn_ref(input_embeddings, router_w, w1, b1, w2, b2):
        import jax, jax.numpy as jnp
        import numpy as np
        NUM_EXPERTS = 8
        TOP_K = 2
        B, S, D = (8, 2048, 64)

        def _moe(tokens, router_w, w1, b1, w2, b2):
            N = tokens.shape[0]
            E = router_w.shape[0]
            logits = tokens.astype(jnp.float32) @ router_w.astype(jnp.float32).T
            probs = jax.nn.softmax(logits, axis=-1)
            rw, re = jax.lax.top_k(probs, TOP_K)
            if TOP_K > 1:
                rw = rw / jnp.maximum(rw.sum(-1, keepdims=True), 1e-12)
            rw = rw.astype(tokens.dtype)
            combine = jnp.zeros((N, E), tokens.dtype).at[jnp.arange(N)[:, None], re].set(rw)
            out = tokens
            for e in range(E):
                h = jax.nn.gelu(tokens @ w1[e] + b1[e], approximate=False)
                y = h @ w2[e] + b2[e]
                out = out + combine[:, e:e + 1] * y
            return out
        b, s, d = input_embeddings.shape
        tokens = input_embeddings.reshape(b * s, d)
        return _moe(tokens, router_w, w1, b1, w2, b2).reshape(b, s, d)

    def _L2_attn_ref(x, Wq, Wk, Wv, Wo):
        import jax, jax.numpy as jnp
        import numpy as np
        H = 4
        TOP_K = 8
        CAUSAL = True
        W_STD = 0.04
        B, T, d = x.shape
        dh = d // H
        k = min(TOP_K, T)
        Q = (x @ Wq.T).reshape(B, T, H, dh).transpose(0, 2, 1, 3)
        K = (x @ Wk.T).reshape(B, T, H, dh).transpose(0, 2, 1, 3)
        V = (x @ Wv.T).reshape(B, T, H, dh).transpose(0, 2, 1, 3)
        scores = jnp.max(Q[:, :, :, None, :] + K[:, :, None, :, :], axis=-1)
        if CAUSAL:
            causal_mask = jnp.triu(jnp.ones((T, T), dtype=bool), 1)
            scores = jnp.where(causal_mask[None, None], -jnp.inf, scores)
        topk_vals, topk_idx = jax.lax.top_k(scores, k)
        attn = jax.nn.softmax(topk_vals, axis=-1)
        Vg = jnp.take_along_axis(V[:, :, None, :, :], topk_idx[..., None], axis=3)
        ctx = jnp.einsum('bhtk,bhtkd->bhtd', attn, Vg)
        ctx = ctx.transpose(0, 2, 1, 3).reshape(B, T, d)
        return ctx @ Wo.T

    def _L2_ffn_ref(x, gamma, beta, Wr, br, W1, b1, W2, b2):
        import jax, jax.numpy as jnp
        import numpy as np
        E = 8
        K = 2
        D = 64
        H = 128
        DOUT = 64
        EPS = 1e-05
        mu = jnp.mean(x, axis=-1, keepdims=True)
        var = jnp.mean(jnp.square(x - mu), axis=-1, keepdims=True)
        xn = (x - mu) * jax.lax.rsqrt(var + EPS) * gamma + beta
        logits = jnp.einsum('bsd,de->bse', xn, Wr) + br
        top_vals, top_idx = jax.lax.top_k(logits, K)
        w = jax.nn.softmax(top_vals, axis=-1)
        w_full = jnp.einsum('bsk,bske->bse', w, jax.nn.one_hot(top_idx, E, dtype=w.dtype))
        y = jnp.zeros(x.shape[:-1] + (DOUT,), x.dtype)
        for e in range(E):
            h = jax.nn.gelu(jnp.einsum('bsd,dh->bsh', xn, W1[e]) + b1[e], approximate=False)
            y_e = jnp.einsum('bsh,hd->bsd', h, W2[e]) + b2[e]
            y = y + y_e * w_full[..., e, None]
        return y

    def _L3_attn_ref(nodes, W):
        import jax, jax.numpy as jnp
        import numpy as np
        F = nodes.shape[-1]
        norm_const = 1.0 / jnp.sqrt(jnp.asarray(F, dtype=nodes.dtype))
        x = jnp.einsum('bnf,fg->bng', nodes, W)
        prods = jnp.einsum('bnf,bmf->bnm', x, nodes)
        att_scores = jax.nn.softmax(prods * norm_const, axis=-1)
        messgs = jnp.einsum('bnm,bmf->bnf', att_scores, nodes)
        return messgs

    def _L3_ffn_ref(x, W1, b1, Wg, bg, Wd, bd):
        import jax, jax.numpy as jnp
        import numpy as np
        C = 64
        HID = 256
        E = 8
        TEMP = 1.0
        orig_shape = x.shape
        xf = x.reshape(-1, orig_shape[-1])
        H = jax.nn.gelu(xf @ W1 + b1, approximate=False)
        probs = jax.nn.softmax((H @ Wg + bg) / TEMP, axis=-1)
        assign = jnp.argmax(probs, axis=-1)
        out = jnp.zeros_like(xf)
        for e in range(Wd.shape[0]):
            y = H @ Wd[e] + bd[e]
            sel = (assign == e)[:, None]
            out = out + jnp.where(sel, probs[:, e:e + 1] * y, 0.0)
        return out.reshape(orig_shape)
    h = _L0_tok_ref(x, L0_tok_W, L0_tok_b)
    h = _layernorm(h + _L0_attn_ref(h, L0_attn_ln_w, L0_attn_ln_b, L0_attn_Wu, L0_attn_bu, L0_attn_Wv, L0_attn_bv, L0_attn_Wbase, L0_attn_bbase, L0_attn_q_w, L0_attn_q_b, L0_attn_k_w, L0_attn_k_b, L0_attn_w_rel, L0_attn_Wo, L0_attn_bo), axis=-1)
    h = _layernorm(h + _L0_ffn_ref(h, L0_ffn_gate_w, L0_ffn_gate_b, L0_ffn_w1, L0_ffn_b1, L0_ffn_w2, L0_ffn_b2), axis=-1)
    h = _layernorm(h + _L1_attn_ref(h, L1_attn_nu_log, L1_attn_theta_log, L1_attn_gamma_log, L1_attn_B_re, L1_attn_B_im, L1_attn_C_re, L1_attn_C_im), axis=-1)
    h = _layernorm(h + _L1_ffn_ref(h, L1_ffn_router_w, L1_ffn_w1, L1_ffn_b1, L1_ffn_w2, L1_ffn_b2), axis=-1)
    h = _layernorm(h + _L2_attn_ref(h, L2_attn_Wq, L2_attn_Wk, L2_attn_Wv, L2_attn_Wo), axis=-1)
    h = _layernorm(h + _L2_ffn_ref(h, L2_ffn_gamma, L2_ffn_beta, L2_ffn_Wr, L2_ffn_br, L2_ffn_W1, L2_ffn_b1, L2_ffn_W2, L2_ffn_b2), axis=-1)
    h = _layernorm(h + _L3_attn_ref(h, L3_attn_W), axis=-1)
    h = _layernorm(h + _L3_ffn_ref(h, L3_ffn_W1, L3_ffn_b1, L3_ffn_Wg, L3_ffn_bg, L3_ffn_Wd, L3_ffn_bd), axis=-1)
    return h

_drawn_inputs = setup_inputs


def setup_inputs(seed=0):
    import zlib

    import numpy as np

    out = dict(_drawn_inputs(seed))
    spreads = {'L0_attn_ln_w': (1.0, 0.6),
     'L0_attn_ln_b': (0.0, 0.8),
     'L0_attn_bu': (0.0, 0.8),
     'L0_attn_bv': (0.0, 0.8),
     'L0_attn_bbase': (0.0, 0.8),
     'L0_attn_q_b': (0.0, 0.8),
     'L0_attn_k_b': (0.0, 0.8),
     'L0_attn_bo': (0.0, 0.1),
     'L0_ffn_gate_b': (0.0, 0.1),
     'L0_ffn_b1': (0.0, 0.356),
     'L0_ffn_b2': (0.0, 0.314),
     'L1_ffn_b1': (0.0, 0.286),
     'L1_ffn_b2': (0.0, 0.1),
     'L2_ffn_br': (0.0, 0.362),
     'L3_ffn_b1': (0.0, 0.8),
     'L3_ffn_bg': (0.0, 0.435),
     'L3_ffn_bd': (0.0, 0.577)}
    factors = {'L0_attn_Wu': 6.002,
     'L0_attn_Wv': 8.0,
     'L0_attn_Wbase': 8.0,
     'L0_attn_q_w': 8.0,
     'L0_attn_k_w': 8.0,
     'L0_attn_w_rel': 6.196,
     'L0_attn_Wo': 3.776,
     'L2_ffn_gamma': 8.0,
     'L2_ffn_beta': 8.0,
     'L2_ffn_Wr': 4.019,
     'L2_ffn_W1': 4.272,
     'L2_ffn_b1': 8.0,
     'L2_ffn_W2': 4.098,
     'L2_ffn_b2': 3.101,
     'L3_ffn_W1': 7.886,
     'L3_ffn_Wg': 8.0,
     'L3_ffn_Wd': 8.0}
    for name, (base, spread) in spreads.items():
        noise = np.random.default_rng([zlib.crc32(name.encode()), seed]).standard_normal(out[name].shape)
        drawn = base * np.exp(spread * noise) if base else spread * noise
        out[name] = jnp.asarray(drawn.astype(out[name].dtype))
    for name, factor in factors.items():
        out[name] = (out[name] * factor).astype(out[name].dtype)
    return out
```

```python
from contextlib import ExitStack

import numpy as np

import concourse.bass as bass
from concourse import mybir

ALU = mybir.AluOpType
ACT = mybir.ActivationFunctionType
AX = mybir.AxisListType.X
F32 = mybir.dt.float32
BF16 = mybir.dt.bfloat16
I32 = mybir.dt.int32

P = 128
IMAGES, SIDE, PATCH, CHANNELS = 16, 96, 16, 3
POS = (SIDE // PATCH) ** 2
TOK = IMAGES * POS
D = 64
TILES = -(-TOK // P)
TOKP = TILES * P
HALF = TOK // 2
IN_K = CHANNELS * PATCH * PATCH // P
E = 8
CAP = -(-5 * TOK // (4 * E))
MPE = 1024
HEADS, DH, TOP = 4, 16, 8
SPAD = 40
NEG = -1.0e30
EPS = 1e-5
FMAX = 3.4028234e38
PI = float(np.pi)

WIDTHS = [
    ("tok_w", IN_K * D), ("tok_b", 1),
    ("ln_w", 1), ("ln_b", 1), ("bu", 1), ("bbase", 1), ("bbase_sw", 1),
    ("q_w", 1), ("q_b", 1), ("q_w_sw", 1), ("q_b_sw", 1), ("k_w", 1), ("k_b", 1), ("k_w_sw", 1), ("k_b_sw", 1),
    ("nu", 1), ("theta", 1), ("gamma_log", 1),
    ("Wu", P), ("Wbase", P), ("Wbase_sw", P), ("Wv", P), ("Wo", D), ("bias_rel", POS),
    ("bv_row", P), ("bo_row", D), ("gb0_row", E), ("br_row", E), ("bg_row", E),
    ("gate_w", E), ("b1_0", 2 * E), ("w1_0", E * P), ("b2_0", D), ("w2_0", 2 * E * D),
    ("lru_b1", P), ("lru_b2", P), ("lru_c1", D), ("lru_c2", D),
    ("router_w", E), ("b1_1", E // 2), ("w1_1", 2 * P), ("b2_1", D), ("w2_1", E // 2 * D),
    ("wq2", P), ("wk", D), ("wv2", D), ("wo2", D),
    ("gam2", 1), ("bet2", 1), ("Wr", E), ("b1_2", E), ("w1_2", E // 2 * P), ("b2_2", D), ("w2_2", E * D),
    ("W3", D), ("b1_3", 2), ("w1_3", P), ("Wg", 2 * E), ("bd", D), ("Wd", 2 * E * D),
]
OFF = {}
_at = 0
for _name, _w in WIDTHS:
    OFF[_name] = (_at, _at + _w)
    _at += _w
WCOLS = _at
GROUPS = {"tok": ("tok_w", "gamma_log"), "a0": ("Wu", "bg_row"), "f0": ("gate_w", "b2_0"), "f0b": ("w2_0", "w2_0"),
          "r1": ("lru_b1", "w2_1"), "r2": ("wq2", "w2_2"), "r3": ("W3", "Wd")}

CONST_WIDTHS = [("ident", P), ("id2", D), ("rope_c", POS), ("rope_s", POS), ("sign", 1), ("first", E),
                ("causal", 8)]
COFF = {}
_at = 0
for _name, _w in CONST_WIDTHS:
    COFF[_name] = (_at, _at + _w)
    _at += _w
CCOLS = _at
BCONST_WIDTHS = [("ones_tri", 2 * P), ("ident", P), ("sel1", E * P), ("sel2", E // 2 * P), ("id2", D),
                 ("selk", TOK)]
BOFF = {}
_at = 0
for _name, _w in BCONST_WIDTHS:
    BOFF[_name] = (_at, _at + _w)
    _at += _w
BCOLS = _at

SEMS = """const tok_w patch0 patch1 patch2 patch3 patch4 patch5 w_a0 w_f0 w_f0b w_r1 w_r2 w_r3
filled tok_acc yt_ready folded res_ready ln_stat ln_aggr ln_eps ln_rstd normed turned ht_ready ht_upper
dve_step act_step pool_step
proj_u proj_base proj_base_sw proj_v silu_u silu_base silu_v rope_in q_ready k_ready qk_done kern_ready
ctx_done uc_ready
logits exp_in exp_out onehot counted comb_split comb_turned comb_t ctf_ready gates z_done act_out gated y_done
lru_exp lru_ang lru_sin lru_u lru_w
qk2 q_parts k_parts k_bounce k_bcast v2_done v2_ready score_mm score_red exp2_in exp2_out prob2 prob2_t
prob2_copied ctx2_done ctx2_ready idrep
x3_done x3_ready s3_done exp3_in exp3_out p3_ready p3_t p3_copied h3_t h3_copied o3_done
h3_ready y3_done y3_used stored""".split()


def tower(nc, patches, weights, consts, bconsts, scratch, out):
    with ExitStack() as ctx:
        def sb(name, shape, dt=F32):
            return ctx.enter_context(nc.sbuf_tensor(name, shape, dt))

        S = {n: ctx.enter_context(nc.semaphore(n)) for n in SEMS}

        X = sb("patch_sb", [P, IN_K, TOK])
        WT = sb("weights_sb", [P, WCOLS])
        CT = sb("consts_sb", [P, CCOLS])
        BT = sb("bconsts_sb", [P, BCOLS], BF16)

        def w(name, rows=P, r0=0):
            a, b = OFF[name]
            return WT[r0:r0 + rows, a:b]

        def c(name, rows=P, r0=0):
            a, b = COFF[name]
            return CT[r0:r0 + rows, a:b]

        def cb(name, rows=P, r0=0):
            a, b = BOFF[name]
            return BT[r0:r0 + rows, a:b]

        H = sb("h", [P, TILES, D])
        XN = sb("xn", [P, TILES, D])
        R = sb("residual", [P, TILES, D])
        HT = sb("hT", [P, TOKP])
        YS = sb("y_sb", [P, TOKP])
        stat = sb("ln_stat_sb", [P, TILES, 6])
        mv = sb("ln_mean_var", [P, TILES, 2])
        ve = sb("ln_var_eps", [P, TILES])
        rstd = sb("ln_rstd_sb", [P, TILES])
        mhalf = sb("minus_half", [P, TILES])
        ones = sb("ones", [1, P])

        U = sb("u_sb", [P, TOK])
        B1 = sb("base_sb", [P, TOK])
        B2 = sb("base_sw_sb", [P, TOK])
        V = sb("v_sb", [P, 8, P])
        QP, QS, KP, KS = (sb(n, [P, TOK]) for n in ("qp", "qs", "kp", "ks"))
        QF = sb("q_rot", [P, TOK])
        K1, K2 = sb("k_rot1", [P, TOKP]), sb("k_rot2", [P, TOKP])
        ST = sb("s_biased", [P, 8, POS])
        KT = sb("kernel_T", [P, 8, POS])
        UC = sb("u_ctx", [P, TOKP])

        lg = sb("logits_sb", [P, TILES, E])
        ex = sb("exp_sb", [P, TILES, E])
        t8 = [sb(f"gate_tmp{i}", [P, TILES, E]) for i in range(4)]
        m5 = [sb(f"gate_col{i}", [P, TILES]) for i in range(5)]
        ohb = sb("onehot_bf", [P, TILES, E], BF16)
        comb = sb("combine", [P, TILES, E])
        comb3 = sb("combine_parts", [P, TILES, 3 * E], BF16)
        CT3 = sb("combine_parts_T", [3 * E, TOKP], BF16)
        CTF = sb("combine_parts_T32", [3 * E, TOKP])
        RING = 4
        HR = sb("hidden", [P, RING, TOK])
        HG = sb("hidden_gated", [P, RING, TOK])
        nf = sb("nonfinite", [P, TILES * D], I32)
        np_, nm = sb("plus_inf", [P, TILES * D]), sb("minus_inf", [P, TILES * D])

        par = sb("lru_par", [P, 8])
        kint = sb("lru_turns", [P, 1], I32)
        ck, sk = sb("lru_cos", [P, POS]), sb("lru_sin_sb", [P, POS])
        tt1, tt2 = sb("lru_t1", [P, POS]), sb("lru_t2", [P, POS])
        Cin, Sin, Cout, Sout = (sb(n, [P, POS]) for n in ("rot_in_c", "rot_in_s", "rot_out_c", "rot_out_s"))
        rr = sb("decay", [P, TOK])
        ua, ub = sb("lru_ua", [P, TOK]), sb("lru_ub", [P, TOK])
        wst = sb("lru_state", [P, TOK])
        WC, WS = sb("lru_wc", [P, TOKP]), sb("lru_ws", [P, TOKP])

        QA = sb("q_parts12", [P, TOK], BF16)
        QB = sb("q_part3_sel", [P, TOK], BF16)
        q1b = sb("q1_tmp", [P, TOK], BF16)
        q2b = sb("q2_tmp", [D, TOK], BF16)
        qres = sb("q_rest", [P, TOK])
        KB = sb("k_parts_img", [P, POS * D], BF16)
        k1f = sb("k_rest", [P, TILES * D])
        kp3 = sb("k_parts_tok", [P, 3, TILES * D], BF16)
        SC = sb("scores", [P, TILES, HEADS, SPAD])
        REP = sb("scores_rest", [P, TILES, HEADS, SPAD])
        PR = sb("probs", [P, TILES, HEADS, 64])
        top = sb("top8", [P, TILES, HEADS, 8])
        d20 = [sb(f"row_stat{i}", [P, TILES * HEADS]) for i in range(2)]
        PT = sb("probs_T", [P, 2, TOKP])
        VB = sb("v_blockdiag", [P, 2 * IMAGES, 2 * DH])
        CX = sb("ctx2_sb", [D, TOKP])

        XT = sb("x3_T", [D, TOKP])
        E3 = sb("exp3_sb", [P, 8, POS])
        r3 = [sb(f"row3_{i}", [P, 8]) for i in range(3)]
        ET = sb("probs3_T", [POS, 8, P])
        HB = sb("h_by_image", [POS, IMAGES, D])
        HH = sb("hidden3", [P, 2, TOKP])
        YM = sb("y3_gated", [P, TILES, E, D])
        YR = sb("y3_sum", [P, TILES, D])

        PS = ctx.enter_context(nc.psum_tensor("ps", [P, 8, 512], F32))

        def two(bank, rows=P, r0=0):
            return PS[r0:r0 + rows, bank:bank + 2, 0:HALF]

        def flat2(bank, n, rows=P):
            return PS[0:rows, bank:bank + 2, :].rearrange("p b f -> p (b f)")[:, 0:n]

        def halves(ap):
            return ap[:, 0:TOK].rearrange("p (h n) -> p h n", h=2)

        ZA, ZB, G, Y, RB = 0, 2, 4, 6, 5
        psR = PS[:, RB, 0:TILES * D].rearrange("p (i d) -> p i d", i=TILES)
        psL = PS[:, RB, 0:TILES * E].rearrange("p (i e) -> p i e", i=TILES)
        psN = PS[:, RB, 64:64 + TILES * E].rearrange("p (i e) -> p i e", i=TILES)
        psCT = PS[0:3 * E, RB, 128:128 + TOKP // 2].bitcast(BF16)

        def tile_cols(i):
            return slice(i * P, (i + 1) * P)

        def img(b):
            return (b % 2) * 64, b // 2

        def over_images(tab):
            return tab.unsqueeze(1).unsqueeze(1).to_broadcast([P, 2, 8, POS])

        def by_image(ap):
            return ap[:, 0:TOK].rearrange("p (h b n) -> p h b n", h=2, b=8)

        FFN = {0: (2 * E, lambda ch: ch // 2), 1: (E // 2, lambda ch: ch), 2: (E, lambda ch: ch)}
        BASE = {0: 0, 1: 2 * E, 2: 2 * E + E // 2}
        GBASE = {0: 0, 1: E, 2: E + E // 2}
        CHUNKS = 2 * E + E // 2 + E

        block = ctx.enter_context(nc.Block())

        @block.sync
        def _(sp):
            def load(group, sem):
                a, b = OFF[GROUPS[group][0]][0], OFF[GROUPS[group][1]][1]
                sp.dma_start(WT[:, a:b], weights[:, a:b]).then_inc(S[sem], 16)

            load("tok", "tok_w")
            for k in range(IN_K):
                sp.dma_start(X[:, k, :], patches[k]).then_inc(S[f"patch{k}"], 16)
            sp.dma_start(CT[:, :], consts).then_inc(S["const"], 16)
            load("a0", "w_a0")
            sp.dma_start(BT[:, :], bconsts).then_inc(S["const"], 16)
            for g in ("f0", "f0b", "r1", "r2", "r3"):
                load(g, "w_" + g)
            sp.wait_ge(S["k_parts"], 3)
            for part in range(3):
                src = kp3[:, part, :].rearrange("p (i e) -> p i e", i=TILES)
                sp.dma_start(scratch[part, 0:4 * P, :].rearrange("(i p) e -> p i e", p=P),
                             src[:, 0:4, :]).then_inc(S["k_bounce"], 16)
                sp.dma_start(scratch[part, 4 * P:TOK, :], src[0:TOK - 4 * P, 4, :]).then_inc(S["k_bounce"], 16)
            sp.wait_ge(S["k_bounce"], 6 * 16)
            sp.dma_start(KB[64:64 + 3 * IMAGES, :],
                         scratch.rearrange("a (b n) e -> (a b) (n e)", b=IMAGES)).then_inc(S["k_bcast"], 16)
            sp.wait_ge(S["normed"], 10 * TILES)
            sp.dma_start(out[0:4 * P, :].rearrange("(i p) e -> p i e", p=P), H[:, 0:4, :]).then_inc(S["stored"], 16)
            sp.dma_start(out[4 * P:TOK, :], H[0:TOK - 4 * P, 4, :]).then_inc(S["stored"], 16)
            sp.wait_ge(S["stored"], 32)

        @block.gpsimd
        def _(pool):
            pool.memset(mhalf[:, :], -0.5).then_inc(S["pool_step"], 1)
            fills = [(ones[:, :], 1.0), (SC[:, :, :, :], NEG), (PR[:, :, :, SPAD:64], 0.0), (VB[:, :, :], 0.0),
                     (HH[:, :, TOK:TOKP], 0.0), (CX[:, TOK:TOKP], 0.0), (XT[:, TOK:TOKP], 0.0)]
            fills += [(t[:, TOK:TOKP], 0.0) for t in (YS, UC, K1, K2, WC, WS)]
            for n, (t, value) in enumerate(fills):
                pool.memset(t, value).then_inc(S["filled"], 1)
                pool.wait_ge(S["filled"], n + 1)
            pool.wait_ge(S["const"], 32)
            pool.tensor_copy(KB[0:64, :].rearrange("p (s e) -> p s e", s=POS),
                             cb("id2", 64).unsqueeze(1).to_broadcast([64, POS, D])).then_inc(S["idrep"], 1)
            pool.wait_ge(S["idrep"], 1)
            pool.tensor_copy(QB[64:64 + 3 * IMAGES, :], cb("selk", 3 * IMAGES, 64)).then_inc(S["idrep"], 1)
            pool.wait_ge(S["pool_step"], 1)
            pool.wait_ge(S["idrep"], 2)
            for k in range(10):
                pool.wait_ge(S["ln_aggr"], TILES * (k + 1))
                pool.tensor_scalar(ve[:, :], mv[:, :, 1], EPS, None, ALU.add).then_inc(S["ln_eps"], 1)
                pool.wait_ge(S["ln_eps"], k + 1)
                pool.tensor_tensor(rstd[:, :], ve[:, :], mhalf[:, :], ALU.pow).then_inc(S["ln_rstd"], 1)
                if k in (1, 3, 6, 8):
                    n = (1, 3, 6, 8).index(k)
                    pool.wait_ge(S["comb_t"], n + 1)
                    pool.tensor_copy(CTF[:, :], CT3[:, :]).then_inc(S["ctf_ready"], 1)

        @block.tensor
        def _(pe):
            mm = pe.matmul

            def fold(n):
                pe.wait_ge(S["yt_ready"], n + 1)
                if n > 0:
                    pe.wait_ge(S["ctf_ready"], n)
                for i in range(TILES):
                    last = mm(psR[:, i, :], YS[:, tile_cols(i)], c("id2"), start=True, stop=(n == 0))
                    if n > 0:
                        last = mm(psR[:, i, :], CTF[:, tile_cols(i)], w(f"b2_{n - 1}", 3 * E), start=False, stop=True)
                last.then_inc(S["folded"], 1)

            def turn(k, src):
                pe.wait_ge(S["normed"], TILES * (k + 1))
                z = flat2(ZA, TOKP, D)
                for i in range(TILES):
                    last = pe.transpose(z[:, tile_cols(i)], src[:, i, :], c("ident"))
                last.then_inc(S["turned"], 1)

            def logits(n, weight, row, chunks=None):
                for i in range(TILES):
                    mm(psL[:, i, :], ones[0:1, :], w(row, 1), start=True, stop=False)
                    if chunks is None:
                        last = mm(psL[:, i, :], HT[0:64, tile_cols(i)], w(weight, 64), start=False, stop=True)
                    else:
                        for ch in range(2):
                            last = mm(psL[:, i, :], HH[:, ch, tile_cols(i)],
                                      w(weight)[:, ch * E:(ch + 1) * E], start=False, stop=(ch == 1))
                last.then_inc(S["logits"], 1)

            def turn_gates(n):
                pe.wait_ge(S["comb_split"], n + 1)
                for i in range(TILES):
                    last = pe.transpose(psCT[:, tile_cols(i)], comb3[:, i, :], cb("ident"))
                last.then_inc(S["comb_turned"], 1)

            def ffn(n):
                chunks, gate_of = FFN[n]
                w1 = w(f"w1_{n}").rearrange("p (c f) -> p c f", f=P)
                w2 = w(f"w2_{n}").rearrange("p (c d) -> p c d", d=D)
                sel = cb("sel1" if n != 1 else "sel2", 3 * E).rearrange("p (g f) -> p g f", f=P)

                def hidden(ch):
                    at = BASE[n] + ch
                    z = ZA if ch % 2 == 0 else ZB
                    if ch >= 2:
                        pe.wait_ge(S["act_out"], at - 1)
                    half = (ch % 2) * 64
                    for j in range(2):
                        last = mm(PS[:, z + j, 0:HALF], w1[half:half + 64, ch // 2, :],
                                  HT[half:half + 64, j * HALF:(j + 1) * HALF], start=True, stop=True)
                    last.then_inc(S["z_done"], 1)

                def gate(g, after):
                    if after > BASE[n]:
                        pe.wait_ge(S["gated"], after)
                    for j in range(2):
                        last = mm(PS[:, G + j, 0:HALF], sel[:, g, :], CT3[:, j * HALF:(j + 1) * HALF],
                                  start=True, stop=True)
                    last.then_inc(S["gates"], 1)

                def down(pair):
                    pe.wait_ge(S["gated"], BASE[n] + 2 * pair + 2)
                    for j in range(2):
                        for ch in (2 * pair, 2 * pair + 1):
                            half = (ch % 2) * 64
                            last = mm(PS[half:half + 64, Y + j, 0:HALF], w2[:, ch, :],
                                      HG[:, ch % RING, j * HALF:(j + 1) * HALF],
                                      start=(pair == 0), stop=(pair == chunks // 2 - 1))
                    last.then_inc(S["y_done"], 1)

                hidden(0)
                pe.wait_ge(S["ht_upper"], n + 1)
                hidden(1)
                if n == 0:
                    pe.wait_ge(S["onehot"], 1)
                    tri = cb("ones_tri").rearrange("p (a t) -> p a t", a=2)
                    for i in range(TILES):
                        for k in range(i + 1):
                            last = mm(psN[:, i, :], tri[:, int(k == i), :], ohb[:, k, :],
                                      start=(k == 0), stop=(k == i))
                    last.then_inc(S["counted"], 1)
                turn_gates(n)
                pe.wait_ge(S["comb_t"], n + 1)
                for pair in range(chunks // 2):
                    for ch in (2 * pair, 2 * pair + 1):
                        if pair > 0:
                            hidden(ch)
                        if gate_of(ch) != gate_of(ch - 1) or ch == 0:
                            gate(gate_of(ch), BASE[n] + ch)
                    if pair > 0:
                        down(pair - 1)
                down(chunks // 2 - 1)

            pe.wait_ge(S["tok_w"], 16)
            pe.wait_ge(S["dve_step"], 1)
            tokw = w("tok_w").rearrange("p (k d) -> p k d", k=IN_K)
            for r in range(IN_K // 2):
                pe.wait_ge(S[f"patch{2 * r}"], 16)
                pe.wait_ge(S[f"patch{2 * r + 1}"], 16)
                for j in range(2):
                    for k in (2 * r, 2 * r + 1):
                        half = (k % 2) * 64
                        last = mm(PS[half:half + 64, Y + j, 0:HALF], tokw[:, k, :], X[:, k, j * HALF:(j + 1) * HALF],
                                  start=(r == 0), stop=(r == IN_K // 2 - 1))
            last.then_inc(S["tok_acc"], 1)
            pe.wait_ge(S["const"], 32)
            pe.wait_ge(S["filled"], 13)
            fold(0)

            turn(0, XN)
            pe.wait_ge(S["w_a0"], 16)
            pe.wait_ge(S["ht_ready"], 1)
            for bank, name, sem in ((ZA, "Wu", "proj_u"), (ZB, "Wbase", "proj_base"), (G, "Wbase_sw", "proj_base_sw")):
                if bank == G:
                    pe.wait_ge(S["res_ready"], 1)
                for j in range(2):
                    last = mm(PS[:, bank + j, 0:HALF], w(name, 64), HT[0:64, j * HALF:(j + 1) * HALF],
                              start=True, stop=True)
                last.then_inc(S[sem], 1)
            for j in range(2):
                mm(PS[:, Y + j, :].rearrange("p (a e) -> p a e", a=4), ones[0:1, :],
                   w("bv_row", 1).unsqueeze(1).to_broadcast([1, 4, P]), start=True, stop=False, skip_group_check=True)
            for b in range(IMAGES):
                r0, q = img(b)
                last = mm(PS[r0:r0 + 64, Y + q // 4, (q % 4) * P:(q % 4 + 1) * P], HT[0:64, b * POS:b * POS + 64],
                          w("Wv", 64), start=False, stop=True, skip_group_check=True)
            last.then_inc(S["proj_v"], 1)
            pe.wait_ge(S["q_ready"], 1)
            pe.wait_ge(S["k_ready"], 2)
            pe.wait_ge(S["silu_u"], 1)
            for b in range(IMAGES):
                r0, q = img(b)
                for t, kk in enumerate((K1, K2)):
                    last = mm(PS[r0:r0 + 64, ZA, q * POS:(q + 1) * POS], kk[:, b * POS:b * POS + 64],
                              QF[:, b * POS:(b + 1) * POS], start=(t == 0), stop=(t == 1))
            last.then_inc(S["qk_done"], 1)
            pe.wait_ge(S["kern_ready"], 1)
            pe.wait_ge(S["silu_v"], 1)
            pe.wait_ge(S["silu_base"], 1)
            for b in range(IMAGES):
                r0, q = img(b)
                last = mm(PS[:, ZB + b % 2, q * POS:(q + 1) * POS], V[r0:r0 + POS, q, :],
                          KT[r0:r0 + POS, q, :], start=True, stop=True)
            last.then_inc(S["ctx_done"], 1)
            pe.wait_ge(S["uc_ready"], 1)
            pe.wait_ge(S["silu_base"], 2)
            for i in range(TILES):
                mm(psR[:, i, :], ones[0:1, :], w("bo_row", 1), start=True, stop=False)
                last = mm(psR[:, i, :], UC[:, tile_cols(i)], w("Wo"), start=False, stop=True)
            last.then_inc(S["folded"], 1)

            turn(1, H)
            pe.wait_ge(S["w_f0"], 16)
            pe.wait_ge(S["w_f0b"], 16)
            pe.wait_ge(S["ht_ready"], 2)
            logits(0, "gate_w", "gb0_row")
            ffn(0)
            fold(1)

            turn(2, H)
            pe.wait_ge(S["w_r1"], 16)
            pe.wait_ge(S["ht_ready"], 3)
            for bank, name in ((ZA, "lru_b1"), (ZB, "lru_b2")):
                for j in range(2):
                    last = mm(PS[:, bank + j, 0:HALF], w(name, 64), HT[0:64, j * HALF:(j + 1) * HALF],
                              start=True, stop=True)
                last.then_inc(S["lru_u"], 1)
            pe.wait_ge(S["lru_w"], 2)
            for i in range(TILES):
                mm(psR[:, i, :], WC[:, tile_cols(i)], w("lru_c1"), start=True, stop=False)
                last = mm(psR[:, i, :], WS[:, tile_cols(i)], w("lru_c2"), start=False, stop=True)
            last.then_inc(S["folded"], 1)

            turn(3, H)
            pe.wait_ge(S["ht_ready"], 4)
            for i in range(TILES):
                last = mm(psL[:, i, :], HT[0:64, tile_cols(i)], w("router_w", 64), start=True, stop=True)
            last.then_inc(S["logits"], 1)
            ffn(1)
            fold(2)

            turn(4, H)
            pe.wait_ge(S["w_r2"], 16)
            pe.wait_ge(S["ht_ready"], 5)
            for i in range(TILES):
                last = mm(PS[:, G, i * D:(i + 1) * D], HT[0:64, tile_cols(i)], w("wk", 64), start=True, stop=True)
            last.then_inc(S["qk2"], 1)
            for j in range(2):
                last = mm(PS[:, ZB + j, 0:HALF], w("wq2", 64), HT[0:64, j * HALF:(j + 1) * HALF],
                          start=True, stop=True)
            last.then_inc(S["qk2"], 1)
            for b in range(IMAGES):
                for h in range(HEADS):
                    r0, at = (h % 2) * 64, (h // 2 * IMAGES + b) * DH
                    last = mm(PS[r0:r0 + SPAD, Y, at:at + DH], HT[0:64, b * POS:b * POS + SPAD],
                              w("wv2", 64)[:, h * DH:(h + 1) * DH], start=True, stop=True)
            last.then_inc(S["v2_done"], 1)
            pe.wait_ge(S["q_parts"], 3)
            pe.wait_ge(S["idrep"], 2)
            pe.wait_ge(S["k_bcast"], 16)
            n = 0
            for j in range(TILES):
                rows = P if j < 4 else TOK - 4 * P
                for g in range(j + 1):
                    keys = min(8, POS - 8 * g)
                    if n >= 4:
                        pe.wait_ge(S["score_red"], n - 3)
                    o = PS[0:rows, n % 4, 0:keys * D].rearrange("p (s e) -> p s e", e=D)
                    mm(o, QA[:, j * P:j * P + rows],
                       cb("id2").unsqueeze(1).to_broadcast([P, keys, D]), start=True, stop=False)
                    mm(PS[0:rows, n % 4, 0:keys * D], QB[0:64 + 3 * IMAGES, j * P:j * P + rows],
                       KB[0:64 + 3 * IMAGES, g * 8 * D:(g * 8 + keys) * D],
                       start=False, stop=True).then_inc(S["score_mm"], 1)
                    n += 1
            pe.wait_ge(S["prob2"], 1)
            for pair in range(2):
                z = flat2(ZA if pair == 0 else ZB, TOKP)
                for j in range(TILES):
                    last = pe.transpose(z[:, tile_cols(j)],
                                        PR[:, j, 2 * pair:2 * pair + 2, :].rearrange("p h s -> p (h s)"), c("ident"))
                last.then_inc(S["prob2_t"], 1)
            pe.wait_ge(S["prob2_copied"], 2)
            pe.wait_ge(S["v2_ready"], 2)
            for b in range(IMAGES):
                for pair in range(2):
                    last = mm(PS[pair * 32:(pair + 1) * 32, G + b // 8, (b % 8) * POS:(b % 8 + 1) * POS],
                              VB[:, pair * IMAGES + b, :], PT[:, pair, b:TOK:IMAGES], start=True, stop=True)
            last.then_inc(S["ctx2_done"], 1)
            pe.wait_ge(S["ctx2_ready"], 1)
            for i in range(TILES):
                last = mm(psR[:, i, :], CX[:, tile_cols(i)], w("wo2", 64), start=True, stop=True)
            last.then_inc(S["folded"], 1)

            turn(6, XN)
            pe.wait_ge(S["ht_ready"], 6)
            logits(2, "Wr", "br_row")
            ffn(2)
            fold(3)

            turn(7, H)
            pe.wait_ge(S["w_r3"], 16)
            pe.wait_ge(S["ht_ready"], 7)
            for j in range(2):
                last = mm(PS[0:64, ZB + j, 0:HALF], w("W3", 64), HT[0:64, j * HALF:(j + 1) * HALF],
                          start=True, stop=True)
            last.then_inc(S["x3_done"], 1)
            for b in range(IMAGES):
                last = pe.transpose(PS[0:POS, Y + b // 8, (b % 8) * D:(b % 8 + 1) * D],
                                    HT[0:64, b * POS:(b + 1) * POS], c("ident", 64)[:, 0:64])
            last.then_inc(S["h3_t"], 1)
            pe.wait_ge(S["x3_ready"], 1)
            for b in range(IMAGES):
                r0, q = img(b)
                last = mm(PS[r0:r0 + 64, ZA, q * POS:(q + 1) * POS], XT[:, b * POS:b * POS + 64],
                          HT[0:64, b * POS:(b + 1) * POS], start=True, stop=True)
            last.then_inc(S["s3_done"], 1)
            pe.wait_ge(S["p3_ready"], 1)
            z = flat2(ZB, 8 * P, POS)
            for q in range(8):
                last = pe.transpose(z[:, q * P:(q + 1) * P], E3[:, q, :], c("ident"))
            last.then_inc(S["p3_t"], 1)
            pe.wait_ge(S["p3_copied"], 1)
            pe.wait_ge(S["h3_copied"], 1)
            for b in range(IMAGES):
                r0, q = img(b)
                last = mm(PS[0:64, G + b // 8, (b % 8) * POS:(b % 8 + 1) * POS], HB[:, b, :],
                          ET[:, q, r0:r0 + POS], start=True, stop=True)
            last.then_inc(S["o3_done"], 1)
            pe.wait_ge(S["ctx2_ready"], 2)
            for i in range(TILES):
                last = mm(psR[:, i, :], CX[:, tile_cols(i)], c("ident", 64)[:, 0:64], start=True, stop=True)
            last.then_inc(S["folded"], 1)

            turn(8, H)
            pe.wait_ge(S["ht_ready"], 8)
            w13 = w("w1_3")
            for ch in range(2):
                if ch == 1:
                    pe.wait_ge(S["ht_upper"], 4)
                for j in range(2):
                    z = ZA if ch == 0 else ZB
                    last = mm(PS[:, z + j, 0:HALF], w13[ch * 64:ch * 64 + 64, :],
                              HT[ch * 64:ch * 64 + 64, j * HALF:(j + 1) * HALF], start=True, stop=True)
                last.then_inc(S["z_done"], 1)
            pe.wait_ge(S["h3_ready"], 2)
            logits(3, "Wg", "bg_row", chunks=2)
            wd = w("Wd").rearrange("p (c f) -> p c f", c=2)
            for i in range(TILES):
                for ch in range(2):
                    last = mm(PS[:, i, :], HH[:, ch, tile_cols(i)], wd[:, ch, :], start=(ch == 0), stop=(ch == 1))
                last.then_inc(S["y3_done"], 1)
            turn_gates(3)
            pe.wait_ge(S["ctf_ready"], 4)
            for i in range(TILES):
                last = mm(psR[:, i, :], CTF[:, tile_cols(i)], w("bd", 3 * E), start=True, stop=True)
            last.then_inc(S["folded"], 1)

        @block.scalar
        def _(act):
            steps = [0]

            def link(ins):
                steps[0] += 1
                ins.then_inc(S["act_step"], 1)
                act.wait_ge(S["act_step"], steps[0])

            def y_evac(n):
                act.activation(halves(YS), two(Y), ACT.Identity,
                               bias=w("tok_b") if n == 0 else 0.0).then_inc(S["yt_ready"], 1)

            def ht_evac(k, count, scale=1.0, bias=0.0):
                act.wait_ge(S["turned"], count)
                act.activation(HT[0:D, :], flat2(ZA, TOKP, D), ACT.Identity, bias=bias, scale=scale)\
                   .then_inc(S["ht_ready"], 1)

            def expo(n):
                act.wait_ge(S["exp_in"], n + 1)
                act.activation(ex[:, :, :], t8[0][:, :, :], ACT.Exp).then_inc(S["exp_out"], 1)

            def hidden(n, func):
                chunks, _ = FFN[n]
                for ch in range(chunks):
                    at = BASE[n] + ch
                    act.wait_ge(S["z_done"], at + 1)
                    if ch >= RING:
                        act.wait_ge(S["gated"], at - RING + 1)
                    act.activation(halves(HR[:, ch % RING, :]), two(ZA if ch % 2 == 0 else ZB), func,
                                   bias=w(f"b1_{n}")[:, ch:ch + 1]).then_inc(S["act_out"], 1)
                    if ch == 1:
                        expo(n)

            act.wait_ge(S["tok_w"], 16)
            link(act.activation(par[:, 0:1], w("nu"), ACT.Exp))
            link(act.activation(par[:, 1:2], par[:, 0:1], ACT.Exp, scale=-1.0))
            act.activation(par[:, 2:3], w("theta"), ACT.Exp).then_inc(S["lru_exp"], 1)
            act.activation(par[:, 3:4], w("gamma_log"), ACT.Exp).then_inc(S["lru_exp"], 1)
            act.wait_ge(S["lru_ang"], 1)
            act.activation(par[:, 5:6], par[:, 4:5], ACT.Sin).then_inc(S["lru_sin"], 1)
            act.activation(par[:, 6:7], par[:, 4:5], ACT.Sin, scale=0.5).then_inc(S["lru_sin"], 1)

            act.wait_ge(S["tok_acc"], 1)
            y_evac(0)

            act.wait_ge(S["w_a0"], 16)
            ht_evac(0, 1, scale=w("ln_w", D), bias=w("ln_b", D))
            act.wait_ge(S["proj_u"], 1)
            act.activation(halves(U), two(ZA), ACT.Silu, bias=w("bu")).then_inc(S["silu_u"], 1)
            act.wait_ge(S["proj_base"], 1)
            act.activation(halves(B1), two(ZB), ACT.Silu, bias=w("bbase")).then_inc(S["silu_base"], 1)
            act.wait_ge(S["proj_base_sw"], 1)
            act.activation(halves(B2), two(G), ACT.Silu, bias=w("bbase_sw")).then_inc(S["silu_base"], 1)
            act.wait_ge(S["proj_v"], 1)
            act.activation(V[:, :, :].rearrange("p q e -> p (q e)"), flat2(Y, 8 * P), ACT.Silu)\
               .then_inc(S["silu_v"], 1)
            act.wait_ge(S["silu_base"], 2)
            for dst, src, nm_ in ((QP, B1, "q_%s"), (QS, B2, "q_%s_sw"), (KP, B1, "k_%s"), (KS, B2, "k_%s_sw")):
                act.activation(dst[:, :], src[:, :], ACT.Identity, bias=w(nm_ % "b"), scale=w(nm_ % "w"))\
                   .then_inc(S["rope_in"], 1)

            ht_evac(1, 2)
            hidden(0, ACT.Relu)
            act.wait_ge(S["y_done"], E)
            y_evac(1)

            ht_evac(2, 3)
            ht_evac(3, 4)
            hidden(1, ACT.Gelu)
            act.wait_ge(S["y_done"], E + E // 4)
            y_evac(2)

            ht_evac(4, 5)
            act.wait_ge(S["exp2_in"], 1)
            act.activation(SC[:, :, :, :], SC[:, :, :, :], ACT.Exp).then_inc(S["exp2_out"], 1)
            act.wait_ge(S["prob2_t"], 2)
            act.activation(PT[:, 1, :], flat2(ZB, TOKP), ACT.Copy).then_inc(S["prob2_copied"], 1)
            act.wait_ge(S["ctx2_done"], 1)
            act.activation(halves(CX), two(G, 64), ACT.Copy).then_inc(S["ctx2_ready"], 1)

            ht_evac(6, 6, scale=w("gam2", D), bias=w("bet2", D))
            hidden(2, ACT.Gelu)
            act.wait_ge(S["y_done"], E + E // 4 + E // 2)
            y_evac(3)

            ht_evac(7, 7)
            act.wait_ge(S["x3_done"], 1)
            act.activation(halves(XT), two(ZB, 64), ACT.Copy).then_inc(S["x3_ready"], 1)
            act.wait_ge(S["h3_t"], 1)
            act.activation(HB[:, :, :].rearrange("p b d -> p (b d)"), flat2(Y, IMAGES * D, POS), ACT.Copy)\
               .then_inc(S["h3_copied"], 1)
            act.wait_ge(S["exp3_in"], 1)
            act.activation(E3[:, :, :], ST[:, :, :], ACT.Exp, scale=float(D) ** -0.5).then_inc(S["exp3_out"], 1)
            act.wait_ge(S["p3_t"], 1)
            act.activation(ET[:, :, :].rearrange("p q t -> p (q t)"), flat2(ZB, 8 * P, POS), ACT.Copy)\
               .then_inc(S["p3_copied"], 1)
            act.wait_ge(S["o3_done"], 1)
            act.activation(halves(CX), two(G, 64), ACT.Copy).then_inc(S["ctx2_ready"], 1)

            ht_evac(8, 8)
            for ch in range(2):
                act.wait_ge(S["z_done"], CHUNKS + ch + 1)
                act.activation(halves(HH[:, ch, :]), two(ZA if ch == 0 else ZB), ACT.Gelu,
                               bias=w("b1_3")[:, ch:ch + 1]).then_inc(S["h3_ready"], 1)
            expo(3)

        @block.vector
        def _(dve):
            steps = [1]

            def step(ins):
                steps[0] += 1
                ins.then_inc(S["dve_step"], 1)

            def sync():
                dve.wait_ge(S["dve_step"], steps[0])

            def link(ins):
                step(ins)
                sync()

            def layernorm(k, src, dst):
                for i in range(TILES):
                    dve.bn_stats(stat[:, i, :], src[:, i, :]).then_inc(S["ln_stat"], 1)
                dve.wait_ge(S["ln_stat"], TILES * (k + 1))
                for i in range(TILES):
                    dve.bn_aggr(mv[:, i, :], stat[:, i, :]).then_inc(S["ln_aggr"], 1)
                dve.wait_ge(S["ln_rstd"], k + 1)
                for i in range(TILES):
                    dve.tensor_scalar(dst[:, i, :], src[:, i, :], mv[:, i, 0:1], rstd[:, i:i + 1],
                                      ALU.subtract, ALU.mult).then_inc(S["normed"], 1)

            def add_residual(n, times=1.0):
                dve.wait_ge(S["folded"], n)
                dve.scalar_tensor_tensor(R[:, :, :].rearrange("p i d -> p (i d)"), H[:, :, :].rearrange("p i d -> p (i d)"),
                                         times, PS[:, RB, 0:TILES * D], ALU.mult, ALU.add).then_inc(S["res_ready"], 1)
                dve.wait_ge(S["res_ready"], n)

            def ht_upper(count):
                dve.wait_ge(S["ht_ready"], count)
                dve.tensor_copy(HT[D:P, :], HT[0:D, :]).then_inc(S["ht_upper"], 1)

            def col(x):
                return x[:, :].unsqueeze(2).to_broadcast([P, TILES, E])

            def take_first(dst, mx, src, tmp, mxi):
                link(dve.tensor_tensor(tmp[:, :, :], src[:, :, :], col(mx), ALU.is_equal))
                link(dve.tensor_tensor(tmp[:, :, :], tmp[:, :, :],
                                       c("first").unsqueeze(1).to_broadcast([P, TILES, E]), ALU.mult))
                link(dve.tensor_reduce(mxi[:, :], tmp[:, :, :], AX, ALU.max))
                link(dve.tensor_tensor(dst[:, :, :], tmp[:, :, :], col(mxi), ALU.is_equal))

            def read_logits(n):
                dve.wait_ge(S["logits"], n + 1)
                link(dve.tensor_copy(lg[:, :, :], psL))
                link(dve.tensor_reduce(m5[0][:, :], lg[:, :, :], AX, ALU.max))
                dve.tensor_tensor(t8[0][:, :, :], lg[:, :, :], col(m5[0]), ALU.subtract).then_inc(S["exp_in"], 1)

            def split_gates(n):
                link(dve.tensor_copy(comb3[:, :, 0:E], comb[:, :, :]))
                link(dve.tensor_tensor(t8[1][:, :, :], comb[:, :, :], comb3[:, :, 0:E], ALU.subtract))
                link(dve.tensor_copy(comb3[:, :, E:2 * E], t8[1][:, :, :]))
                dve.tensor_tensor(comb3[:, :, 2 * E:3 * E], t8[1][:, :, :], comb3[:, :, E:2 * E],
                                  ALU.subtract).then_inc(S["comb_split"], 1)
                dve.wait_ge(S["comb_turned"], n + 1)
                dve.tensor_copy(CT3[:, :], psCT).then_inc(S["comb_t"], 1)

            def top1(n, kept):
                read_logits(n)
                take_first(t8[2], m5[0], lg, t8[1], m5[1])
                if kept:
                    dve.tensor_copy(ohb[:, :, :], t8[2][:, :, :]).then_inc(S["onehot"], 1)
                dve.wait_ge(S["exp_out"], n + 1)
                link(dve.tensor_reduce(m5[2][:, :], ex[:, :, :], AX, ALU.add))
                link(dve.reciprocal(m5[3][:, :], m5[2][:, :]))
                link(dve.tensor_tensor(comb[:, :, :], t8[2][:, :, :], col(m5[3]), ALU.mult))
                if kept:
                    dve.wait_ge(S["counted"], 1)
                    link(dve.tensor_scalar(t8[1][:, :, :], psN, CAP + 0.5, None, ALU.is_lt))
                    link(dve.tensor_tensor(comb[:, :, :], comb[:, :, :], t8[1][:, :, :], ALU.mult))
                split_gates(n)

            def top2(n):
                read_logits(n)
                take_first(t8[2], m5[0], lg, t8[1], m5[1])
                link(dve.scalar_tensor_tensor(lg[:, :, :], t8[2][:, :, :], NEG, lg[:, :, :], ALU.mult, ALU.add))
                link(dve.tensor_reduce(m5[0][:, :], lg[:, :, :], AX, ALU.max))
                take_first(t8[3], m5[0], lg, t8[1], m5[1])
                link(dve.tensor_tensor(t8[2][:, :, :], t8[2][:, :, :], t8[3][:, :, :], ALU.add))
                dve.wait_ge(S["exp_out"], n + 1)
                link(dve.tensor_tensor(t8[2][:, :, :], t8[2][:, :, :], ex[:, :, :], ALU.mult))
                link(dve.tensor_reduce(m5[2][:, :], t8[2][:, :, :], AX, ALU.add))
                link(dve.reciprocal(m5[3][:, :], m5[2][:, :]))
                link(dve.tensor_tensor(comb[:, :, :], t8[2][:, :, :], col(m5[3]), ALU.mult))
                split_gates(n)

            def gate_hidden(n):
                chunks, gate_of = FFN[n]
                for ch in range(chunks):
                    at = BASE[n] + ch
                    dve.wait_ge(S["act_out"], at + 1)
                    dve.wait_ge(S["gates"], GBASE[n] + gate_of(ch) + 1)
                    if ch >= RING:
                        dve.wait_ge(S["y_done"], BASE[n] // 2 + (ch - RING) // 2 + 1)
                    dve.tensor_tensor(halves(HG[:, ch % RING, :]), halves(HR[:, ch % RING, :]), two(G), ALU.mult)\
                       .then_inc(S["gated"], 1)

            dve.memset(PS[:, :, :], 0.0).then_inc(S["dve_step"], 1)

            dve.wait_ge(S["lru_exp"], 2)
            dve.wait_ge(S["const"], 32)
            link(dve.tensor_scalar(par[:, 4:5], par[:, 2:3], 1.0 / (2 * PI), None, ALU.mult))
            link(dve.tensor_copy(kint[:, :], par[:, 4:5]))
            link(dve.tensor_copy(par[:, 7:8], kint[:, :]))
            hi = float(np.float32(6.28125))
            link(dve.scalar_tensor_tensor(par[:, 4:5], par[:, 7:8], -hi, par[:, 2:3], ALU.mult, ALU.add))
            link(dve.scalar_tensor_tensor(par[:, 4:5], par[:, 7:8], -(2 * PI - hi), par[:, 4:5], ALU.mult, ALU.add))
            dve.tensor_scalar(par[:, 4:5], par[:, 4:5], 3.1415925, -3.1415925, ALU.min, ALU.max)\
               .then_inc(S["lru_ang"], 1)
            step(dve.memset(ck[:, 0:1], 1.0))
            step(dve.memset(sk[:, 0:1], 0.0))
            step(dve.memset(rr[:, :], 1.0))
            sync()
            step(dve.memset(rr[:, 0:TOK:POS], 0.0))
            sync()
            link(dve.tensor_scalar(rr[:, :], rr[:, :], par[:, 1:2], None, ALU.mult))
            dve.wait_ge(S["lru_sin"], 2)
            step(dve.tensor_copy(sk[:, 1:2], par[:, 5:6]))
            link(dve.tensor_scalar(tt1[:, 0:1], par[:, 6:7], par[:, 6:7], -2.0, ALU.mult, ALU.mult))
            link(dve.tensor_scalar(ck[:, 1:2], tt1[:, 0:1], 1.0, None, ALU.add))
            known = 1
            while known < POS - 1:
                n = min(known, POS - 1 - known)
                cz, sz = ck[:, known:known + 1], sk[:, known:known + 1]
                cj, sj = ck[:, 1:n + 1], sk[:, 1:n + 1]
                step(dve.tensor_scalar(tt1[:, 0:n], sj, sz, None, ALU.mult))
                step(dve.tensor_scalar(tt2[:, 0:n], sj, cz, None, ALU.mult))
                sync()
                step(dve.scalar_tensor_tensor(ck[:, known + 1:known + n + 1], cj, cz, tt1[:, 0:n],
                                              ALU.mult, ALU.subtract))
                step(dve.scalar_tensor_tensor(sk[:, known + 1:known + n + 1], cj, sz, tt2[:, 0:n],
                                              ALU.mult, ALU.add))
                sync()
                known += n
            step(dve.tensor_scalar(Cin[:, :], ck[:, :], par[:, 3:4], None, ALU.mult))
            step(dve.tensor_scalar(Sin[:, :], sk[:, :], par[:, 3:4], c("sign"), ALU.mult, ALU.mult))
            step(dve.tensor_scalar(Cout[:, :], ck[:, :], c("sign"), None, ALU.mult))
            step(dve.tensor_scalar(Sout[:, :], sk[:, :], -1.0, None, ALU.mult))

            dve.wait_ge(S["folded"], 1)
            dve.tensor_copy(H[:, :, :], psR).then_inc(S["res_ready"], 1)
            dve.wait_ge(S["res_ready"], 1)
            layernorm(0, H, XN)

            tab_c = c("rope_c").unsqueeze(1).to_broadcast([P, IMAGES, POS])
            tab_s = c("rope_s").unsqueeze(1).to_broadcast([P, IMAGES, POS])

            def parity(x):
                return x[:, 0:TOK].rearrange("p (q a n) -> p a q n", a=2, n=POS)

            def imgs(x):
                return x[:, 0:TOK].rearrange("p (b n) -> p b n", b=IMAGES)

            dve.wait_ge(S["rope_in"], 1)
            step(dve.tensor_tensor(imgs(QP), imgs(QP), tab_c, ALU.mult))
            dve.wait_ge(S["rope_in"], 2)
            link(dve.tensor_tensor(imgs(QS), imgs(QS), tab_s, ALU.mult))
            dve.tensor_tensor(QF[:, :], QP[:, :], QS[:, :], ALU.add).then_inc(S["q_ready"], 1)
            dve.wait_ge(S["rope_in"], 3)
            dve.wait_ge(S["filled"], 13)
            dve.tensor_tensor(imgs(K1), imgs(KP), tab_c, ALU.mult).then_inc(S["k_ready"], 1)
            dve.wait_ge(S["rope_in"], 4)
            dve.tensor_tensor(imgs(K2), imgs(KS), tab_s, ALU.mult).then_inc(S["k_ready"], 1)
            dve.wait_ge(S["qk_done"], 1)
            s8 = PS[:, ZA, 0:8 * POS].rearrange("p (q m) -> p q m", q=8)
            link(dve.scalar_tensor_tensor(ST[:, :, :], s8, 1.0 / MPE,
                                          w("bias_rel").unsqueeze(1).to_broadcast([P, 8, POS]), ALU.mult, ALU.add))
            dve.scalar_tensor_tensor(KT[:, :, :], ST[:, :, :], 0.0, ST[:, :, :], ALU.max, ALU.mult)\
               .then_inc(S["kern_ready"], 1)
            dve.wait_ge(S["silu_u"], 1)
            dve.wait_ge(S["ctx_done"], 1)
            dve.tensor_tensor(parity(UC), parity(U), two(ZB).rearrange("p a (q n) -> p a q n", q=8), ALU.mult).then_inc(S["uc_ready"], 1)
            add_residual(2)
            layernorm(1, R, H)

            ht_upper(2)
            top1(0, kept=True)
            gate_hidden(0)
            dve.wait_ge(S["folded"], 3)
            rf = R[:, :, :].rearrange("p i d -> p (i d)")
            link(dve.tensor_copy(rf, PS[:, RB, 0:TILES * D]))
            step(dve.tensor_scalar(np_[:, :], rf, FMAX, 1.0e4, ALU.is_gt, ALU.mult))
            step(dve.tensor_scalar(nm[:, :], rf, -FMAX, 1.0e4, ALU.is_lt, ALU.mult))
            step(dve.tensor_scalar(nf[:, :], rf, 0.0, 0.0, ALU.mult, ALU.not_equal))
            sync()
            link(dve.tensor_tensor(np_[:, :], np_[:, :], nm[:, :], ALU.subtract))
            link(dve.copy_predicated(rf, nf[:, :], np_[:, :]))
            dve.tensor_tensor(R[:, :, :], H[:, :, :], R[:, :, :], ALU.add).then_inc(S["res_ready"], 1)
            dve.wait_ge(S["res_ready"], 3)
            layernorm(2, R, H)

            dve.wait_ge(S["lru_u"], 1)
            step(dve.tensor_tensor(by_image(ua), two(ZA).rearrange("p h (b n) -> p h b n", b=8),
                                   over_images(Cin[:, :]), ALU.mult))
            dve.wait_ge(S["lru_u"], 2)
            link(dve.tensor_tensor(by_image(ub), two(ZB).rearrange("p h (b n) -> p h b n", b=8),
                                   over_images(Sin[:, :]), ALU.mult))
            link(dve.tensor_tensor(ua[:, :], ua[:, :], ub[:, :], ALU.add))
            link(dve.tensor_tensor_scan(wst[:, :], rr[:, :], ua[:, :], 0.0, ALU.mult, ALU.add))
            dve.tensor_tensor(by_image(WC), by_image(wst), over_images(Cout[:, :]), ALU.mult).then_inc(S["lru_w"], 1)
            dve.tensor_tensor(by_image(WS), by_image(wst), over_images(Sout[:, :]), ALU.mult).then_inc(S["lru_w"], 1)
            add_residual(4)
            layernorm(3, R, H)

            ht_upper(4)
            top2(1)
            gate_hidden(1)
            add_residual(5, times=2.0)
            layernorm(4, R, H)

            dve.wait_ge(S["qk2"], 1)
            psK = PS[:, G, 0:TILES * D]
            dve.tensor_copy(kp3[:, 0, :], psK).then_inc(S["k_parts"], 1)
            dve.wait_ge(S["k_parts"], 1)
            link(dve.tensor_tensor(k1f[:, :], psK, kp3[:, 0, :], ALU.subtract))
            dve.tensor_copy(kp3[:, 1, :], k1f[:, :]).then_inc(S["k_parts"], 1)
            dve.wait_ge(S["k_parts"], 2)
            dve.tensor_tensor(kp3[:, 2, :], k1f[:, :], kp3[:, 1, :], ALU.subtract).then_inc(S["k_parts"], 1)
            dve.wait_ge(S["qk2"], 2)
            psQ = two(ZB)
            link(dve.tensor_copy(halves(q1b), psQ))
            step(dve.tensor_tensor(halves(qres), psQ, halves(q1b), ALU.subtract))

            def pos_major(x, r0):
                return x[r0:r0 + 64, :].rearrange("p (n b) -> p b n", b=IMAGES)

            def img_major(x, r0):
                return x[r0:r0 + 64, :].rearrange("p (b n) -> p b n", b=IMAGES)

            dve.tensor_copy(pos_major(QA, 0), img_major(q1b, 0)).then_inc(S["q_parts"], 1)
            sync()
            dve.tensor_copy(pos_major(QA, 64), img_major(qres, 64)).then_inc(S["q_parts"], 1)
            link(dve.tensor_copy(q2b[:, :], qres[0:64, :]))
            dve.tensor_tensor(pos_major(QB, 0), img_major(qres, 0), img_major(q2b, 0), ALU.subtract)\
               .then_inc(S["q_parts"], 1)
            dve.wait_ge(S["v2_done"], 1)
            for h in range(2):
                dve.tensor_copy(VB[64 * h:64 * h + SPAD, :, h * DH:(h + 1) * DH],
                                PS[64 * h:64 * h + SPAD, Y, :].rearrange("p (b e) -> p b e", e=DH))\
                   .then_inc(S["v2_ready"], 1)
            n = 0
            for j in range(TILES):
                rows = P if j < 4 else TOK - 4 * P
                for g in range(j + 1):
                    keys = min(8, POS - 8 * g)
                    dve.wait_ge(S["score_mm"], n + 1)
                    dve.tensor_reduce(SC[0:rows, j, :, 8 * g:8 * g + keys].rearrange("p h s -> p s h"),
                                      PS[0:rows, n % 4, 0:keys * D].rearrange("p (s h d) -> p s h d", h=HEADS, d=DH),
                                      AX, ALU.max).then_inc(S["score_red"], 1)
                    n += 1
                    dve.wait_ge(S["score_red"], n)
            for j in range(TILES):
                diag = SC[:, j, :, 8 * j:8 * j + 8]
                step(dve.tensor_tensor(diag, diag, c("causal").unsqueeze(1).to_broadcast([P, HEADS, 8]), ALU.add))
            sync()
            for j in range(TILES):
                for h in range(HEADS):
                    step(dve.max(top[:, j, h, :], SC[:, j, h, :]))
            sync()
            for j in range(TILES):
                for h in range(HEADS):
                    step(dve.match_replace(REP[:, j, h, :], top[:, j, h, :], SC[:, j, h, :], 2 * NEG))
            sync()
            sc20 = SC[:, :, :, :].rearrange("p j h s -> p (j h) s")
            rep20 = REP[:, :, :, :].rearrange("p j h s -> p (j h) s")
            pr20 = PR[:, :, :, 0:SPAD].rearrange("p j h s -> p (j h) s")

            def row20(x):
                return x.unsqueeze(2).to_broadcast([P, TILES * HEADS, SPAD])

            step(dve.tensor_tensor(rep20, sc20, rep20, ALU.not_equal))
            dve.tensor_tensor(sc20, sc20, row20(top[:, :, :, 0].rearrange("p j h -> p (j h)")), ALU.subtract)\
               .then_inc(S["exp2_in"], 1)
            sync()
            dve.wait_ge(S["exp2_out"], 1)
            link(dve.tensor_tensor(pr20, sc20, rep20, ALU.mult))
            link(dve.tensor_reduce(d20[0][:, :], pr20, AX, ALU.add))
            link(dve.reciprocal(d20[1][:, :], d20[0][:, :]))
            dve.tensor_tensor(pr20, pr20, row20(d20[1][:, :]), ALU.mult).then_inc(S["prob2"], 1)
            dve.wait_ge(S["prob2_t"], 1)
            dve.tensor_copy(PT[:, 0, :], flat2(ZA, TOKP)).then_inc(S["prob2_copied"], 1)
            add_residual(6)
            layernorm(5, R, H)

            dve.wait_ge(S["normed"], 6 * TILES)
            layernorm(6, H, XN)
            ht_upper(6)
            top2(2)
            gate_hidden(2)
            add_residual(7)
            layernorm(7, R, H)

            dve.wait_ge(S["s3_done"], 1)

            def row3(x):
                return x[:, :].unsqueeze(2).to_broadcast([P, 8, POS])

            link(dve.tensor_reduce(r3[0][:, :], s8, AX, ALU.max))
            dve.tensor_tensor(ST[:, :, :], s8, row3(r3[0]), ALU.subtract).then_inc(S["exp3_in"], 1)
            dve.wait_ge(S["exp3_out"], 1)
            link(dve.tensor_reduce(r3[1][:, :], E3[:, :, :], AX, ALU.add))
            link(dve.reciprocal(r3[2][:, :], r3[1][:, :]))
            dve.tensor_tensor(E3[:, :, :], E3[:, :, :], row3(r3[2]), ALU.mult).then_inc(S["p3_ready"], 1)
            add_residual(8)
            layernorm(8, R, H)

            ht_upper(8)
            top1(3, kept=False)
            for i in range(TILES):
                dve.wait_ge(S["y3_done"], i + 1)
                link(dve.tensor_tensor(YM[:, i, :, :], PS[:, i, :].rearrange("p (e d) -> p e d", e=E),
                                       comb[:, i, :].unsqueeze(2).to_broadcast([P, E, D]), ALU.mult))
                step(dve.tensor_reduce(YR[:, i, :], YM[:, i, :, :].rearrange("p e d -> p d e"), AX, ALU.add))
            sync()
            step(dve.tensor_tensor(H[:, :, :], H[:, :, :], YR[:, :, :], ALU.add))
            sync()
            add_residual(9)
            layernorm(9, R, H)


def _constants():
    cst = np.zeros((P, CCOLS), np.float32)
    bcs = np.zeros((P, BCOLS), np.float32)

    def put(dst, off, name, a):
        s, e = off[name]
        dst[:a.shape[0], s:e] = a.reshape(a.shape[0], -1)

    eye, eye64 = np.eye(P, dtype=np.float32), np.eye(D, dtype=np.float32)
    put(cst, COFF, "ident", eye)
    put(cst, COFF, "id2", np.concatenate([eye64, eye64]))
    half = P // 2
    freq = 10000.0 ** (-np.arange(half) / half)
    ang = (freq[:, None] * np.arange(POS)[None, :])
    put(cst, COFF, "rope_c", np.concatenate([np.cos(ang), np.cos(ang)]))
    put(cst, COFF, "rope_s", np.concatenate([-np.sin(ang), np.sin(ang)]))
    put(cst, COFF, "sign", np.concatenate([np.ones((64, 1)), -np.ones((64, 1))]))
    put(cst, COFF, "first", np.tile(E - np.arange(E), (P, 1)))
    own = np.arange(P) // IMAGES
    put(cst, COFF, "causal", np.where(np.arange(8)[None, :] <= own[:, None], 0.0, NEG))
    put(bcs, BOFF, "ones_tri", np.stack([np.ones((P, P)), np.triu(np.ones((P, P)))], 1))
    put(bcs, BOFF, "ident", eye)
    sel = np.zeros((E, E, P))
    sel[np.arange(E), np.arange(E), :] = 1
    put(bcs, BOFF, "sel1", np.tile(sel, (3, 1, 1)))
    sel = np.zeros((E, E // 2, P))
    for e in range(E):
        sel[e, e // 2, (e % 2) * D:(e % 2 + 1) * D] = 1
    put(bcs, BOFF, "sel2", np.tile(sel, (3, 1, 1)))
    put(bcs, BOFF, "id2", np.concatenate([eye64, eye64]))
    s, e = BOFF["selk"]
    bcs[64:64 + 3 * IMAGES, s:e] = np.tile(np.eye(IMAGES), (3, POS))
    return cst, bcs.astype(mybir.dt.np(BF16))


def _pack(i):
    pk = np.zeros((P, WCOLS), np.float32)

    def put(name, a, r0=0):
        s, e = OFF[name]
        pk[r0:r0 + a.shape[0], s:e] = a.reshape(a.shape[0], -1)

    def col(name, a):
        put(name, a.reshape(-1, 1))

    def both(name, a):
        put(name, a)
        put(name, a, 64)

    def swap(a):
        return np.concatenate([a[..., 64:], a[..., :64]], -1)

    put("tok_w", i["L0_tok_W"].T.reshape(IN_K, P, D).transpose(1, 0, 2))
    col("tok_b", i["L0_tok_b"])
    both("ln_w", i["L0_attn_ln_w"].reshape(-1, 1))
    both("ln_b", i["L0_attn_ln_b"].reshape(-1, 1))
    col("bu", i["L0_attn_bu"])
    col("bbase", i["L0_attn_bbase"])
    col("bbase_sw", swap(i["L0_attn_bbase"]))
    for n in ("q_w", "q_b", "k_w", "k_b"):
        col(n, i["L0_attn_" + n][0])
        col(n + "_sw", swap(i["L0_attn_" + n][0]))
    both("nu", i["L1_attn_nu_log"].reshape(-1, 1))
    both("theta", i["L1_attn_theta_log"].reshape(-1, 1))
    both("gamma_log", i["L1_attn_gamma_log"].reshape(-1, 1))
    put("Wu", i["L0_attn_Wu"])
    put("Wbase", i["L0_attn_Wbase"])
    put("Wbase_sw", swap(i["L0_attn_Wbase"]))
    put("Wv", i["L0_attn_Wv"])
    put("Wo", i["L0_attn_Wo"])
    at = np.arange(POS)
    both("bias_rel", i["L0_attn_w_rel"][MPE - 1 + at[:, None] - at[None, :]])
    put("bv_row", i["L0_attn_bv"].reshape(1, -1))
    put("bo_row", i["L0_attn_bo"].reshape(1, -1))
    put("gb0_row", i["L0_ffn_gate_b"].reshape(1, -1))
    put("br_row", i["L2_ffn_br"].reshape(1, -1))
    put("bg_row", i["L3_ffn_bg"].reshape(1, -1))

    def by_half(w1):
        return np.concatenate([w1[:, 0::2], w1[:, 1::2]])

    put("gate_w", i["L0_ffn_gate_w"])
    put("b1_0", i["L0_ffn_b1"].reshape(2 * E, P).T)
    put("w1_0", by_half(i["L0_ffn_w1"].transpose(1, 0, 2).reshape(D, 2 * E, P)))
    put("b2_0", np.tile(i["L0_ffn_b2"], (3, 1)))
    put("w2_0", i["L0_ffn_w2"].reshape(2 * E, P, D).transpose(1, 0, 2))
    br, bi = i["L1_attn_B_re"].T, i["L1_attn_B_im"].T
    put("lru_b1", np.concatenate([br, bi], 1))
    put("lru_b2", np.concatenate([bi, br], 1))
    cr, ci = i["L1_attn_C_re"].T, i["L1_attn_C_im"].T
    put("lru_c1", np.concatenate([cr, ci]))
    put("lru_c2", np.concatenate([ci, cr]))
    put("router_w", i["L1_ffn_router_w"].T)
    put("b1_1", i["L1_ffn_b1"].reshape(E // 2, P).T)
    put("w1_1", by_half(i["L1_ffn_w1"].transpose(1, 0, 2).reshape(D, E // 2, P)))
    put("b2_1", np.tile(i["L1_ffn_b2"], (3, 1)))
    put("w2_1", i["L1_ffn_w2"].reshape(E // 2, P, D).transpose(1, 0, 2))
    put("wq2", np.concatenate([i["L2_attn_Wq"].T, i["L2_attn_Wq"].T], 1))
    put("wk", i["L2_attn_Wk"].T)
    put("wv2", i["L2_attn_Wv"].T)
    put("wo2", i["L2_attn_Wo"].T)
    both("gam2", i["L2_ffn_gamma"].reshape(-1, 1))
    both("bet2", i["L2_ffn_beta"].reshape(-1, 1))
    put("Wr", i["L2_ffn_Wr"])
    put("b1_2", i["L2_ffn_b1"].T)
    put("w1_2", by_half(i["L2_ffn_W1"].transpose(1, 0, 2)))
    put("b2_2", np.tile(i["L2_ffn_b2"], (3, 1)))
    put("w2_2", i["L2_ffn_W2"].transpose(1, 0, 2))
    put("W3", i["L3_attn_W"])
    put("b1_3", i["L3_ffn_b1"].reshape(2, P).T)
    put("w1_3", by_half(i["L3_ffn_W1"].reshape(D, 2, P)))
    put("Wg", i["L3_ffn_Wg"].reshape(2, P, E).transpose(1, 0, 2))
    put("bd", np.tile(i["L3_ffn_bd"], (3, 1)))
    put("Wd", i["L3_ffn_Wd"].reshape(E, 2, P, D).transpose(2, 1, 0, 3))
    return pk


def kernel(**inputs):
    import concourse.bacc as bacc
    from concourse.bass_utils import run_bass_kernel_spmd as run

    i = {k: np.asarray(v) for k, v in inputs.items()}
    side = SIDE // PATCH
    x = i["x"].reshape(IMAGES, CHANNELS, side, PATCH, side, PATCH).transpose(1, 3, 5, 0, 2, 4)
    cst, bcs = _constants()
    arrays = {
        "patches": np.ascontiguousarray(x.reshape(IN_K, P, TOK)),
        "weights": _pack(i),
        "consts": cst,
        "bconsts": bcs,
    }
    nc = bacc.Bacc("TRN2", target_bir_lowering=False, num_devices=1)
    args = [nc.dram_tensor(n, a.shape, mybir.dt.from_np(a.dtype), kind="ExternalInput").ap()
            for n, a in arrays.items()]
    scratch = nc.dram_tensor("k_scratch", (3, TOK, D), BF16, kind="Internal").ap()
    out = nc.dram_tensor("out_0", (TOK, D), F32, kind="ExternalOutput").ap()
    tower(nc, *args, scratch, out)
    r = run(nc, [arrays], core_ids=[0])
    return r.results[0]["out_0"].reshape(IMAGES, POS, D)
```
